# Optimizing a Trainium2 kernel written in Bass

```python
import numpy as np
import jax
import jax.numpy as jnp

def _softmax(x, axis=-1):
    return jax.nn.softmax(x, axis=axis)
def _gelu(x):
    return jax.nn.gelu(x, approximate=True)
def _silu(x):
    return jax.nn.silu(x)
def _sigmoid(x):
    return jax.nn.sigmoid(x)
def _layernorm(x, axis=-1, eps=1e-5):
    m = jnp.mean(x, axis=axis, keepdims=True)
    v = jnp.var(x, axis=axis, keepdims=True)
    return (x - m) / jnp.sqrt(v + eps)
def _scatter_add(tgt, idx, src, axis=0):
    return tgt.at[idx].add(src)
def _segment_sum(src, seg, n):
    return jax.ops.segment_sum(src, seg, n)

kernel_name = 'mk_conv_preact_d1_conv_nhwc96_5fd00b'

def setup_inputs(seed: int = 0):
    np.random.seed(seed)
    _w = jnp.asarray
    def _rec_inputs():
        import jax
        import jax.numpy as jnp
        _gk = jax.random.key(seed)
        x = -0.0001476 + 0.9999 * jax.random.normal(jax.random.fold_in(_gk, 1), (32, 112, 112, 96), jnp.float32)
        return x
    x = _rec_inputs()
    def _L0_conv_setup():
        import jax, jax.numpy as jnp
        from jax import lax
        import numpy as np
        B, H, W, CH, N = (32, 112, 112, 96, 5)
        key = jax.random.key(seed)
        k1, k2 = jax.random.split(key)
        x = jax.random.normal(k1, (B, H, W, CH), dtype=jnp.float32)
        kernel = jax.random.normal(k2, (N, N, CH), dtype=jnp.float32)
        alpha = jnp.ones((1, 1), dtype=jnp.float32)
        bias = jnp.ones((1, 1), dtype=jnp.float32)
        return {'x': x, 'kernel': kernel, 'alpha': alpha, 'bias': bias}
    _L0_conv_all = _L0_conv_setup()
    _L0_conv_in = {k: v for k, v in _L0_conv_all.items() if k in ('kernel', 'alpha', 'bias', )}
    del _L0_conv_all

    return {
        "x": x,
        "L0_conv_kernel": _L0_conv_in["kernel"],
        "L0_conv_alpha": _L0_conv_in["alpha"],
        "L0_conv_bias": _L0_conv_in["bias"],
    }

def reference(x, L0_conv_kernel, L0_conv_alpha, L0_conv_bias):
    import jax
    import jax.numpy as jnp
    def _L0_conv_ref(x, kernel, alpha, bias):
        import jax, jax.numpy as jnp
        from jax import lax
        import numpy as np
        B, H, W, CH, N = (32, 112, 112, 96, 5)
        ch = x.shape[-1]
        rhs = kernel[:, :, None, :]
        conv = lax.conv_general_dilated(x, rhs, window_strides=(1, 1), padding='SAME', dimension_numbers=('NHWC', 'HWIO', 'NHWC'), feature_group_count=ch)
        gate = conv * alpha[0, 0] + bias[0, 0]
        return gate * x + x

    def _gn(v, G=32, eps=1e-5):
        B_, H_, W_, C_ = v.shape
        g = v.reshape(B_, H_, W_, G, C_ // G)
        m = jnp.mean(g, axis=(1, 2, 4), keepdims=True)
        s = jnp.var(g, axis=(1, 2, 4), keepdims=True)
        return ((g - m) / jnp.sqrt(s + eps)).reshape(v.shape)

    def _ln_c(v, eps=1e-6):
        m = jnp.mean(v, axis=-1, keepdims=True)
        s = jnp.var(v, axis=-1, keepdims=True)
        return (v - m) / jnp.sqrt(s + eps)

    def _ln_t(v, eps=1e-5):
        m = jnp.mean(v, axis=-1, keepdims=True)
        s = jnp.var(v, axis=-1, keepdims=True)
        return (v - m) / jnp.sqrt(s + eps)

    def _to_tokens(v):
        B_, H_, W_, C_ = v.shape
        return v.reshape(B_, H_ * W_, C_)
    def _from_tokens(t, like):
        return t.reshape(like.shape)

    x = x + _L0_conv_ref(_gn(x), L0_conv_kernel, L0_conv_alpha, L0_conv_bias)
    return x


_drawn_inputs = setup_inputs


def setup_inputs(seed=0):
    import zlib

    import numpy as np

    out = dict(_drawn_inputs(seed))
    spreads = {}
    factors = {}
    for name, (base, spread) in spreads.items():
        noise = np.random.default_rng([zlib.crc32(name.encode()), seed]).standard_normal(out[name].shape)
        drawn = base * np.exp(spread * noise) if base else spread * noise
        out[name] = jnp.asarray(drawn.astype(out[name].dtype))
    for name, factor in factors.items():
        out[name] = (out[name] * factor).astype(out[name].dtype)
    return out
```

```python
from contextlib import ExitStack

import concourse.bass as bass
from concourse import mybir

IMAGES, HEIGHT, WIDTH, CHANNELS = 32, 112, 112, 96
TAPS = 5
HALO = TAPS // 2
GROUPS = 32
GROUP_CH = CHANNELS // GROUPS
EPS = 1e-5

P = 128
COLS = 4
ROWS = P // COLS - 2 * HALO
STRIPS = HEIGHT // ROWS
PATCHES = WIDTH // COLS
HALF = P // 2
HALO_PARTS = HALO * COLS
MAIN_PARTS = HALF - HALO_PARTS

QUARTER = 4
QUARTERS = 4
UNIT_IMAGES = QUARTER * QUARTERS
UNITS = GROUPS * (IMAGES // UNIT_IMAGES)
UNITS_PER_GROUP = IMAGES // UNIT_IMAGES
COLUMNS = STRIPS * PATCHES
STRIPES = QUARTER * STRIPS
PADDED = PATCHES + 2
TILES = QUARTERS * GROUP_CH
TILE_COLS = STRIPES * PATCHES

X_SLOTS = 4
G_SLOTS = 2
W_SLOTS = 2
BANKS = 6
BN = 6
BN_COUNT = GROUP_CH * COLUMNS // 2
MAIN_TOTAL = 2 * MAIN_PARTS


def build(nc, x_in, taps_in, alpha_in, bias_in, averaging_in, out):
    fp32 = mybir.dt.float32
    ALU = mybir.AluOpType
    ACT = mybir.ActivationFunctionType

    with ExitStack() as ctx:
        def sb(name, shape):
            return ctx.enter_context(nc.sbuf_tensor(name, shape, fp32))

        def sem(name):
            return ctx.enter_context(nc.semaphore(name))

        x = sb("x", [P, X_SLOTS, QUARTERS, GROUP_CH, QUARTER, COLUMNS])
        g = sb("g", [P, G_SLOTS, QUARTERS, GROUP_CH, STRIPES, PADDED])
        taps = sb("taps", [P, W_SLOTS, GROUP_CH, 2, 2, HALF])
        zeros = sb("zeros", [P, GROUP_CH * QUARTER * PATCHES])
        averaging = sb("averaging", [P, 2, P])
        alpha = sb("alpha", [P, 1])
        bias = sb("bias", [P, 1])
        bias_plus_one = sb("bias_plus_one", [P, 1])
        moments = sb("moments", [P, UNIT_IMAGES, 2, BN // 2])
        mean_sum = sb("mean_sum", [P, UNIT_IMAGES])
        offset = sb("offset", [P, UNIT_IMAGES, 2])
        offset_sq = sb("offset_sq", [P, UNIT_IMAGES, 2])
        squares = sb("squares", [P, UNIT_IMAGES, 2])
        square_sum = sb("square_sum", [P, UNIT_IMAGES])
        var_eps = sb("var_eps", [P, UNIT_IMAGES])
        std = sb("std", [P, UNIT_IMAGES])
        rstd_raw = sb("rstd_raw", [P, UNIT_IMAGES])
        newton_a = sb("newton_a", [P, UNIT_IMAGES])
        newton_b = sb("newton_b", [P, UNIT_IMAGES])
        newton_c = sb("newton_c", [P, UNIT_IMAGES])
        rstd = sb("rstd", [P, UNIT_IMAGES])
        shift = sb("shift", [P, UNIT_IMAGES])

        conv = [ctx.enter_context(nc.psum_tensor(f"conv{n}", [P, 512], fp32)) for n in range(BANKS)]
        mean_ps = ctx.enter_context(nc.psum_tensor("mean_ps", [P, 512], fp32))
        var_ps = ctx.enter_context(nc.psum_tensor("var_ps", [P, 512], fp32))

        x_loaded = [[sem(f"x_loaded{s}_{q}") for q in range(QUARTERS)] for s in range(X_SLOTS)]
        x_stored = [[sem(f"x_stored{s}_{q}") for q in range(QUARTERS)] for s in range(X_SLOTS)]
        taps_loaded = [sem(f"taps_loaded{s}") for s in range(W_SLOTS)]
        constants_loaded = sem("constants_loaded")
        cleared = sem("cleared")
        bias_ready = sem("bias_ready")
        taps_scaled = sem("taps_scaled")
        mean_sum_ready = sem("mean_sum_ready")
        mean_ready = sem("mean_ready")
        square_sum_ready = sem("square_sum_ready")
        var_ready = sem("var_ready")
        var_eps_ready = sem("var_eps_ready")
        std_ready = sem("std_ready")
        coefficients_ready = sem("coefficients_ready")
        dve_step = sem("dve_step")
        normalized = sem("normalized")
        g_ready = sem("g_ready")
        tile_convolved = sem("tile_convolved")
        bank_gated = [sem(f"bank_gated{n}") for n in range(BANKS)]
        quarter_added = [sem(f"quarter_added{s}") for s in range(G_SLOTS)]

        class Unit:

            def __init__(self, i, k):
                i, k = i + k // X_SLOTS, k % X_SLOTS
                self.number = i * X_SLOTS + k
                self.x_slot, self.x_visit = k, i
                self.g_slot, self.g_visit = k % G_SLOTS, i * (X_SLOTS // G_SLOTS) + k // G_SLOTS
                self.group_start = k % UNITS_PER_GROUP == 0
                self.w_slot = k // UNITS_PER_GROUP
                self.w_visit = i
                self.group = i * (X_SLOTS // UNITS_PER_GROUP) + k // UNITS_PER_GROUP

            def bank(self, tile):
                at = self.x_slot * TILES + tile
                return at % BANKS, self.x_visit * (X_SLOTS * TILES // BANKS) + at // BANKS

        LAST = UNITS // X_SLOTS - 1

        def x_image(unit, image):
            q, b = divmod(image, QUARTER)
            return x[:, unit.x_slot, q, :, b, :]

        def wait_unless_zero(engine, semaphore, count):
            if not (isinstance(count, int) and count == 0):
                engine.wait_ge(semaphore, count)

        block = ctx.enter_context(nc.Block())

        @block.sync
        def _(sp):
            def load(unit):
                for q in range(QUARTERS):
                    wait_unless_zero(sp, x_stored[unit.x_slot][q], unit.x_visit * 32)
                    sp.dma_start(x[:, unit.x_slot, q].rearrange("p c b n -> p (c b n)"),
                                 x_in[bass.ds(unit.number, 1), :, q, :].rearrange("o p n -> (o p) n")
                                 ).then_inc(x_loaded[unit.x_slot][q], 16)

            def load_taps(unit):
                if not (isinstance(unit.number, int) and unit.group < W_SLOTS):
                    sp.wait_ge(tile_convolved, (unit.number - W_SLOTS * UNITS_PER_GROUP + UNITS_PER_GROUP) * TILES)
                sp.dma_start(taps[:, unit.w_slot].rearrange("p c t s m -> p (c t s m)"),
                             taps_in[bass.ds(unit.group, 1), :, :].rearrange("o p n -> (o p) n")
                             ).then_inc(taps_loaded[unit.w_slot], 16)

            def store(unit):
                for q in range(QUARTERS):
                    sp.wait_ge(quarter_added[unit.g_slot], unit.g_visit * QUARTERS + q + 1)
                    for half in range(2):
                        first = half * HALF + HALO_PARTS
                        sp.dma_start(out[bass.ds(unit.number, 1), half * MAIN_PARTS:(half + 1) * MAIN_PARTS, q, :]
                                     .rearrange("o p n -> (o p) n"),
                                     x[first:first + MAIN_PARTS, unit.x_slot, q].rearrange("p c b n -> p (c b n)")
                                     ).then_inc(x_stored[unit.x_slot][q], 16)

            sp.dma_start(averaging[:], averaging_in).then_inc(constants_loaded, 16)
            sp.dma_start(alpha[:], alpha_in.to_broadcast([P, 1])).then_inc(constants_loaded, 16)
            sp.dma_start(bias[:], bias_in.to_broadcast([P, 1])).then_inc(constants_loaded, 16)
            load(Unit(0, 0))
            load_taps(Unit(0, 0))
            load(Unit(0, 1))

            def phase(i, k, last=False):
                if not last or k + 2 < X_SLOTS:
                    ahead = Unit(i, k + 2)
                    if ahead.group_start:
                        load_taps(ahead)
                    load(ahead)
                store(Unit(i, k))

            for k in range(X_SLOTS):
                phase(0, k)
            with sp.Fori(1, LAST) as i:
                for k in range(X_SLOTS):
                    phase(i, k)
            for k in range(X_SLOTS):
                phase(LAST, k, last=True)
            for slot in range(X_SLOTS):
                for q in range(QUARTERS):
                    sp.wait_ge(x_stored[slot][q], 32 * (LAST + 1))

        @block.scalar
        def _(act):
            def scale_taps(unit):
                act.wait_ge(taps_loaded[unit.w_slot], (unit.w_visit + 1) * 16)
                w = taps[:, unit.w_slot].rearrange("p c t s m -> p (c t s m)")
                nc.scalar.activation(w, w, ACT.Copy, scale=alpha[:, 0:1]).then_inc(taps_scaled, 1)

            def root(unit):
                act.wait_ge(var_eps_ready, unit.number + 1)
                nc.scalar.activation(std[:], var_eps[:], ACT.Sqrt).then_inc(std_ready, 1)

            def normalize(unit):
                act.wait_ge(coefficients_ready, unit.number + 1)
                wait_unless_zero(act, quarter_added[unit.g_slot], unit.g_visit * QUARTERS)
                for q in range(QUARTERS):
                    for b in range(QUARTER):
                        image = q * QUARTER + b
                        last = nc.scalar.activation(
                            g[:, unit.g_slot, q, :, b * STRIPS:(b + 1) * STRIPS, 1:1 + PATCHES],
                            x_image(unit, image).rearrange("p c (s j) -> p c s j", s=STRIPS),
                            ACT.Identity, scale=rstd[:, image:image + 1], bias=shift[:, image:image + 1])
                    last.then_inc(normalized, 1)
                    act.wait_ge(normalized, unit.number * QUARTERS + q + 1)
                    for half, strip in ((0, 0), (1, STRIPS - 1)):
                        lanes = slice(half * HALF, half * HALF + HALO_PARTS)
                        last = nc.scalar.activation(
                            g[lanes, unit.g_slot, q, :, strip::STRIPS, 1:1 + PATCHES],
                            zeros[lanes, :].rearrange("p (c b j) -> p c b j", c=GROUP_CH, b=QUARTER), ACT.Copy)
                    last.then_inc(g_ready, 1)

            act.wait_ge(constants_loaded, 48)
            act.wait_ge(cleared, 2)
            scale_taps(Unit(0, 0))
            root(Unit(0, 0))
            normalize(Unit(0, 0))

            def phase(i, k):
                ahead = Unit(i, k + 1)
                if ahead.group_start:
                    scale_taps(ahead)
                root(ahead)
                normalize(ahead)

            for k in range(X_SLOTS):
                phase(0, k)
            with act.Fori(1, LAST) as i:
                for k in range(X_SLOTS):
                    phase(i, k)
            for k in range(X_SLOTS - 1):
                phase(LAST, k)

        @block.vector
        def _(dve):
            STEPS = 9

            def statistics(unit, image):
                q, b = divmod(image, QUARTER)
                if b == 0:
                    dve.wait_ge(x_loaded[unit.x_slot][q], (unit.x_visit + 1) * 16)
                return nc.vector.bn_stats(moments[:, image].rearrange("p e n -> p (e n)"), x_image(unit, image))

            def step(unit, n, instruction):
                instruction.then_inc(dve_step, 1)
                dve.wait_ge(dve_step, unit.number * STEPS + n)

            def sum_means(unit):
                step(unit, 1, statistics(unit, UNIT_IMAGES - 1))
                nc.vector.tensor_tensor(mean_sum[:], moments[:, :, 0, 1], moments[:, :, 1, 1],
                                        ALU.add).then_inc(mean_sum_ready, 1)

            def sum_squares(unit):
                dve.wait_ge(mean_ready, unit.number + 1)
                mean = mean_ps[:, 0:UNIT_IMAGES].unsqueeze(2).to_broadcast([P, UNIT_IMAGES, 2])
                step(unit, 2, nc.vector.tensor_tensor(offset[:], moments[:, :, :, 1], mean, ALU.subtract))
                step(unit, 3, nc.vector.tensor_tensor(offset_sq[:], offset[:], offset[:], ALU.mult))
                step(unit, 4, nc.vector.scalar_tensor_tensor(squares[:], offset_sq[:], float(BN_COUNT),
                                                             moments[:, :, :, 2], ALU.mult, ALU.add))
                nc.vector.tensor_tensor(square_sum[:], squares[:, :, 0], squares[:, :, 1],
                                        ALU.add).then_inc(square_sum_ready, 1)

            def add_eps(unit):
                dve.wait_ge(var_ready, unit.number + 1)
                nc.vector.tensor_scalar(var_eps[:], var_ps[:, 0:UNIT_IMAGES], EPS, None,
                                        ALU.add).then_inc(var_eps_ready, 1)

            def coefficients(unit):
                dve.wait_ge(std_ready, unit.number + 1)
                wait_unless_zero(dve, g_ready, unit.number * QUARTERS)
                step(unit, 5, nc.vector.reciprocal(rstd_raw[:], std[:]))
                step(unit, 6, nc.vector.tensor_tensor(newton_a[:], rstd_raw[:], rstd_raw[:], ALU.mult))
                step(unit, 7, nc.vector.tensor_tensor(newton_b[:], newton_a[:], var_eps[:], ALU.mult))
                step(unit, 8, nc.vector.tensor_scalar(newton_c[:], newton_b[:], -0.5, 1.5, ALU.mult, ALU.add))
                step(unit, 9, nc.vector.tensor_tensor(rstd[:], newton_c[:], rstd_raw[:], ALU.mult))
                nc.vector.scalar_tensor_tensor(shift[:], mean_ps[:, 0:UNIT_IMAGES], -1.0, rstd[:],
                                               ALU.mult, ALU.mult).then_inc(coefficients_ready, 1)

            def gate(unit, tile):
                q, c = divmod(tile, GROUP_CH)
                bank, _ = unit.bank(tile)
                dve.wait_ge(tile_convolved, unit.number * TILES + tile + 1)
                gq = g[:, unit.g_slot, q, c, :, 1:1 + PATCHES]
                nc.vector.scalar_tensor_tensor(
                    gq, conv[bank][:, 0:TILE_COLS].rearrange("p (s j) -> p s j", j=PATCHES),
                    bias_plus_one[:, 0:1], gq, ALU.add, ALU.mult).then_inc(bank_gated[bank], 1)

            nc.vector.memset(zeros[:], 0.0).then_inc(cleared, 1)
            nc.vector.memset(g[:].rearrange("p a q c s j -> p (a q c s j)"), 0.0).then_inc(cleared, 1)
            dve.wait_ge(constants_loaded, 48)
            nc.vector.tensor_scalar(bias_plus_one[:], bias[:], 1.0, None, ALU.add).then_inc(bias_ready, 1)
            dve.wait_ge(bias_ready, 1)
            for image in range(UNIT_IMAGES - 1):
                statistics(Unit(0, 0), image)
            first = Unit(0, 0)

            def finish(unit):
                sum_means(unit)
                sum_squares(unit)
                add_eps(unit)
                coefficients(unit)

            finish(first)

            PER_TILE = 3

            def phase(i, k, last=False):
                unit = Unit(i, k)
                ahead = None if last and k == X_SLOTS - 1 else Unit(i, k + 1)
                image = 0
                for tile in range(TILES):
                    gate(unit, tile)
                    if ahead is None:
                        continue
                    for _ in range(PER_TILE):
                        if image < UNIT_IMAGES - 1:
                            statistics(ahead, image)
                            image += 1
                    if tile == 5:
                        sum_means(ahead)
                    if tile == 6:
                        sum_squares(ahead)
                    if tile == 7:
                        add_eps(ahead)
                        coefficients(ahead)

            for k in range(X_SLOTS):
                phase(0, k)
            with dve.Fori(1, LAST) as i:
                for k in range(X_SLOTS):
                    phase(i, k)
            for k in range(X_SLOTS):
                phase(LAST, k, last=True)

        @block.tensor
        def _(pe):
            def average(unit, which, ready, source, target, done):
                pe.wait_ge(ready, unit.number + 1)
                nc.tensor.matmul(target[:, 0:UNIT_IMAGES], averaging[:, which, :], source[:],
                                 start=True, stop=True).then_inc(done, 1)

            def average_means(unit):
                average(unit, 0, mean_sum_ready, mean_sum, mean_ps, mean_ready)

            def average_squares(unit):
                average(unit, 1, square_sum_ready, square_sum, var_ps, var_ready)

            def convolve(unit, tile):
                q, c = divmod(tile, GROUP_CH)
                bank, held = unit.bank(tile)
                if c == 0:
                    pe.wait_ge(g_ready, unit.number * QUARTERS + q + 1)
                wait_unless_zero(pe, bank_gated[bank], held)
                for stream in range(2):
                    for half in range(2):
                        j = stream + half
                        last = nc.tensor.matmul(
                            conv[bank][half * HALF:(half + 1) * HALF, 0:TILE_COLS],
                            taps[:, unit.w_slot, c, half, stream, :],
                            g[:, unit.g_slot, q, c, :, j:j + PATCHES],
                            start=stream == 0, stop=stream == 1)
                last.then_inc(tile_convolved, 1)

            pe.wait_ge(constants_loaded, 48)
            average_means(Unit(0, 0))
            average_squares(Unit(0, 0))

            def phase(i, k, last=False):
                unit = Unit(i, k)
                ahead = None if last and k == X_SLOTS - 1 else Unit(i, k + 1)
                if unit.group_start:
                    pe.wait_ge(taps_scaled, unit.group + 1)
                for tile in range(TILES):
                    convolve(unit, tile)
                    if ahead is not None and tile == 6:
                        average_means(ahead)
                    if ahead is not None and tile == 7:
                        average_squares(ahead)

            for k in range(X_SLOTS):
                phase(0, k)
            with pe.Fori(1, LAST) as i:
                for k in range(X_SLOTS):
                    phase(i, k)
            for k in range(X_SLOTS):
                phase(LAST, k, last=True)

        @block.gpsimd
        def _(pool):
            def add(unit):
                for q in range(QUARTERS):
                    bank, held = unit.bank(q * GROUP_CH + GROUP_CH - 1)
                    pool.wait_ge(bank_gated[bank], held + 1)
                    xq = x[:, unit.x_slot, q].rearrange("p c b (s j) -> p (c b s) j", j=PATCHES)
                    tq = g[:, unit.g_slot, q, :, :, 1:1 + PATCHES].rearrange("p c s j -> p (c s) j")
                    nc.gpsimd.tensor_tensor(xq, xq, tq, ALU.add).then_inc(quarter_added[unit.g_slot], 1)

            for k in range(X_SLOTS):
                add(Unit(0, k))
            with pool.Fori(1, LAST) as i:
                for k in range(X_SLOTS):
                    add(Unit(i, k))
            for k in range(X_SLOTS):
                add(Unit(LAST, k))



def _lay_out_x(x):
    import numpy as np
    padded = np.zeros((IMAGES, HEIGHT + 2 * HALO, WIDTH, CHANNELS), x.dtype)
    padded[:, HALO:HALO + HEIGHT] = x

    def rows(first, count):
        at = [HALO + s * ROWS + first for s in range(STRIPS)]
        a = np.stack([padded[:, r:r + count] for r in at], 1)
        return a.reshape(UNITS_PER_GROUP, QUARTERS, QUARTER, STRIPS, count, PATCHES, COLS, GROUPS, GROUP_CH)

    def order(a, row_first):
        a = a.transpose((7, 0, 4, 6, 1, 8, 2, 3, 5) if row_first else (7, 0, 6, 4, 1, 8, 2, 3, 5))
        return a.reshape(UNITS, a.shape[2] * a.shape[3], QUARTERS, GROUP_CH * QUARTER * COLUMNS)

    main = rows(0, ROWS)
    result = np.empty((UNITS, P, QUARTERS, GROUP_CH * QUARTER * COLUMNS), x.dtype)
    result[:, 0:HALO_PARTS] = order(rows(-HALO, HALO), True)
    result[:, HALO_PARTS:HALF] = order(main[..., 0:COLS // 2, :, :], False)
    result[:, HALF:HALF + HALO_PARTS] = order(rows(ROWS, HALO), True)
    result[:, HALF + HALO_PARTS:] = order(main[..., COLS // 2:, :, :], False)
    return result


def _partition_pixels():
    top = [(r - HALO, w, False) for r in range(HALO) for w in range(COLS)]
    left = [(r, w, True) for w in range(COLS // 2) for r in range(ROWS)]
    bottom = [(ROWS + r, w, False) for r in range(HALO) for w in range(COLS)]
    right = [(r, w, True) for w in range(COLS // 2, COLS) for r in range(ROWS)]
    return top + left + bottom + right


def _lay_out_taps(kernel):
    import numpy as np
    pixels = _partition_pixels()
    result = np.zeros((P, 2, 2, HALF, CHANNELS), kernel.dtype)
    for half in range(2):
        for stream in range(2):
            patch = stream + half - 1
            for m in range(HALF):
                row, col, own = pixels[half * HALF + m]
                if not own:
                    continue
                for k, (in_row, in_col, _) in enumerate(pixels):
                    dy, dx = in_row - row + HALO, patch * COLS + in_col - col + HALO
                    if 0 <= dy < TAPS and 0 <= dx < TAPS:
                        result[k, half, stream, m] = kernel[dy, dx]
    result = result.reshape(P, 2, 2, HALF, GROUPS, GROUP_CH).transpose(4, 0, 5, 1, 2, 3)
    return np.ascontiguousarray(result).reshape(GROUPS, P, GROUP_CH * 2 * 2 * HALF)


def _averaging():
    import numpy as np
    result = np.zeros((P, 2, P), np.float32)
    for k, (_, _, own) in enumerate(_partition_pixels()):
        if own:
            result[k, 0] = 1.0 / (2 * MAIN_TOTAL)
            result[k, 1] = 1.0 / (2 * MAIN_TOTAL * BN_COUNT)
    return result


def _restore(out):
    import numpy as np
    a = out.reshape(GROUPS, UNITS_PER_GROUP, COLS, ROWS, QUARTERS, GROUP_CH, QUARTER, STRIPS, PATCHES)
    a = a.transpose(1, 4, 6, 7, 3, 8, 2, 0, 5)
    return np.ascontiguousarray(a).reshape(IMAGES, HEIGHT, WIDTH, CHANNELS)


def kernel(x, L0_conv_kernel, L0_conv_alpha, L0_conv_bias):
    import numpy as np
    import concourse.bacc as bacc
    from concourse.bass_utils import run_bass_kernel_spmd

    arrays = {
        "x_in": _lay_out_x(np.asarray(x)),
        "taps_in": _lay_out_taps(np.asarray(L0_conv_kernel)),
        "alpha_in": np.ascontiguousarray(L0_conv_alpha),
        "bias_in": np.ascontiguousarray(L0_conv_bias),
        "averaging_in": _averaging(),
    }
    nc = bacc.Bacc("TRN2", target_bir_lowering=False, num_devices=1)
    ins = [nc.dram_tensor(n, a.shape, mybir.dt.from_np(a.dtype), kind="ExternalInput").ap()
           for n, a in arrays.items()]
    shape = (UNITS, MAIN_TOTAL, QUARTERS, GROUP_CH * QUARTER * COLUMNS)
    out = nc.dram_tensor("out", shape, mybir.dt.float32, kind="ExternalOutput").ap()
    build(nc, *ins, out)
    result = run_bass_kernel_spmd(nc, [arrays], core_ids=[0])
    return _restore(np.asarray(result.results[0]["out"]))
```

```python
from contextlib import ExitStack

import concourse.bass as bass
from concourse import mybir

IMAGES, HEIGHT, WIDTH, CHANNELS = 32, 112, 112, 96
TAPS = 5
HALO = TAPS // 2
GROUPS = 32
GROUP_CH = CHANNELS // GROUPS
EPS = 1e-5

P = 128
COLS = 4
ROWS = P // COLS - 2 * HALO
STRIPS = HEIGHT // ROWS
PATCHES = WIDTH // COLS
HALF = P // 2
HALO_PARTS = HALO * COLS
MAIN_PARTS = HALF - HALO_PARTS

QUARTER = 4
QUARTERS = 4
UNIT_IMAGES = QUARTER * QUARTERS
UNITS = GROUPS * (IMAGES // UNIT_IMAGES)
UNITS_PER_GROUP = IMAGES // UNIT_IMAGES
COLUMNS = STRIPS * PATCHES
STRIPES = QUARTER * STRIPS
PADDED = PATCHES + 2
TILES = QUARTERS * GROUP_CH
RUN = 512 // STRIPES

X_SLOTS = 4
G_SLOTS = 2
W_SLOTS = 2
SPLIT = 2
SPLIT_QUARTERS = QUARTERS - SPLIT
TAP_BITS = 12
G_SCALE = 256.0
PSUM_SLOTS = 2
BN = 6
BN_COUNT = GROUP_CH * COLUMNS // 2
MAIN_TOTAL = 2 * MAIN_PARTS


def build(nc, x_in, taps_in, tap_list_in, alpha_in, bias_in, matrices_in, out):
    fp32, fp16, int32 = mybir.dt.float32, mybir.dt.float16, mybir.dt.int32
    AXIS = mybir.AxisListType
    ALU = mybir.AluOpType
    ACT = mybir.ActivationFunctionType

    with ExitStack() as ctx:
        def sb(name, shape, dtype=fp32):
            return ctx.enter_context(nc.sbuf_tensor(name, shape, dtype))

        def sem(name):
            return ctx.enter_context(nc.semaphore(name))

        x = sb("x", [P, X_SLOTS, QUARTERS, GROUP_CH, QUARTER, COLUMNS])
        g = sb("g", [P, G_SLOTS, QUARTERS, GROUP_CH, STRIPES, PADDED])
        taps = sb("taps", [P, W_SLOTS, GROUP_CH, 2, 2, HALF])
        zeros = sb("zeros", [P, GROUP_CH * QUARTER * PATCHES])
        g_high = sb("g_high", [P, G_SLOTS, SPLIT_QUARTERS, GROUP_CH, STRIPES, PADDED], fp16)
        g_low = sb("g_low", [P, SPLIT_QUARTERS, GROUP_CH, STRIPES, PADDED], fp16)
        taps_high = sb("taps_high", [P, W_SLOTS, GROUP_CH, 2, 2, HALF], fp16)
        taps_low = sb("taps_low", [P, W_SLOTS, GROUP_CH, 2, 2, HALF], fp16)
        matrices = sb("matrices", [P, 3, P])
        ones = sb("ones", [CHANNELS, P])
        alpha = sb("alpha", [P, 1])
        bias = sb("bias", [P, 1])
        tap_list = sb("tap_list", [CHANNELS, TAPS * TAPS])
        alpha_tap_list = sb("alpha_tap_list", [CHANNELS, TAPS * TAPS])
        channel_max = sb("channel_max", [CHANNELS, 1])
        channel_max_diagonal = sb("channel_max_diagonal", [CHANNELS, CHANNELS])
        largest = sb("largest", [P, 1])
        bounded = sb("bounded", [P, 1])
        bounded_root = sb("bounded_root", [P, 1])
        power = sb("power", [P, 1])
        r = sb("r", [P, 1])
        r_inverse = sb("r_inverse", [P, 1])
        r_squared = sb("r_squared", [P, 1])
        r_squared_inverse = sb("r_squared_inverse", [P, 1])
        bias_plus_one = sb("bias_plus_one", [P, 1])
        tap_scale = sb("tap_scale", [P, 1])
        gate_bias = sb("gate_bias", [P, 1])
        gate_bias_split = sb("gate_bias_split", [P, 1])
        g_restore = sb("g_restore", [P, 1])
        rstd_scale = sb("rstd_scale", [P, UNIT_IMAGES])
        moments = sb("moments", [P, G_SLOTS, UNIT_IMAGES, 2, BN // 2])
        offset = sb("offset", [P, UNIT_IMAGES, 2])
        mean_sum = sb("mean_sum", [P, UNIT_IMAGES])
        offset_sq = sb("offset_sq", [P, UNIT_IMAGES, 2])
        squares = sb("squares", [P, UNIT_IMAGES, 2])
        square_sum = sb("square_sum", [P, UNIT_IMAGES])
        eps = sb("eps", [P, 1])
        std = sb("std", [P, UNIT_IMAGES])
        rstd_raw = sb("rstd_raw", [P, UNIT_IMAGES])
        rstd_scaled = sb("rstd_scaled", [P, UNIT_IMAGES])
        newton_a = sb("newton_a", [P, UNIT_IMAGES])
        newton_b = sb("newton_b", [P, UNIT_IMAGES])
        rstd = sb("rstd", [P, G_SLOTS, UNIT_IMAGES])
        shift = sb("shift", [P, G_SLOTS, UNIT_IMAGES])

        conv = [ctx.enter_context(nc.psum_tensor(f"conv{n}", [P, GROUP_CH, STRIPES, RUN], fp32))
                for n in range(PSUM_SLOTS)]
        mean_ps = ctx.enter_context(nc.psum_tensor("mean_ps", [P, 512], fp32))
        var_ps = ctx.enter_context(nc.psum_tensor("var_ps", [P, 512], fp32))

        x_loaded = [[sem(f"x_loaded{s}_{q}") for q in range(QUARTERS)] for s in range(X_SLOTS)]
        x_stored = [[sem(f"x_stored{s}_{q}") for q in range(QUARTERS)] for s in range(X_SLOTS)]
        taps_loaded = [sem(f"taps_loaded{s}") for s in range(W_SLOTS)]
        constants_loaded = sem("constants_loaded")
        cleared = sem("cleared")
        setup_step = sem("setup_step")
        channel_max_ready = sem("channel_max_ready")
        channel_max_spread = sem("channel_max_spread")
        bounded_ready = sem("bounded_ready")
        bounded_root_ready = sem("bounded_root_ready")
        scales_ready = sem("scales_ready")
        taps_scaled = sem("taps_scaled")
        taps_rounded = sem("taps_rounded")
        taps_split = sem("taps_split")
        mean_sum_ready = sem("mean_sum_ready")
        mean_ready = sem("mean_ready")
        square_sum_ready = sem("square_sum_ready")
        var_ready = sem("var_ready")
        std_ready = sem("std_ready")
        coefficients_ready = sem("coefficients_ready")
        dve_step = sem("dve_step")
        normalized = sem("normalized")
        g_ready = sem("g_ready")
        g_rounded = sem("g_rounded")
        g_split = sem("g_split")
        quarter_convolved = sem("quarter_convolved")
        quarter_gated = [sem(f"quarter_gated{n}") for n in range(PSUM_SLOTS)]
        quarter_added = [sem(f"quarter_added{s}") for s in range(G_SLOTS)]

        class Unit:

            def __init__(self, i, k):
                i, k = i + k // X_SLOTS, k % X_SLOTS
                self.number = i * X_SLOTS + k
                self.x_slot, self.x_visit = k, i
                self.g_slot, self.g_visit = k % G_SLOTS, i * (X_SLOTS // G_SLOTS) + k // G_SLOTS
                self.group_start = k % UNITS_PER_GROUP == 0
                self.w_slot = k // UNITS_PER_GROUP
                self.w_visit = i
                self.group = i * (X_SLOTS // UNITS_PER_GROUP) + k // UNITS_PER_GROUP

            def psum(self, quarter):
                at = self.x_slot * QUARTERS + quarter
                return at % PSUM_SLOTS, self.x_visit * (X_SLOTS * QUARTERS // PSUM_SLOTS) + at // PSUM_SLOTS

        LAST = UNITS // X_SLOTS - 1

        def x_image(unit, image):
            q, b = divmod(image, QUARTER)
            return x[:, unit.x_slot, q, :, b, :]

        def wait_unless_zero(engine, semaphore, count):
            if not (isinstance(count, int) and count == 0):
                engine.wait_ge(semaphore, count)

        block = ctx.enter_context(nc.Block())

        @block.sync
        def _(sp):
            def load(unit, quarters=range(QUARTERS)):
                for q in quarters:
                    wait_unless_zero(sp, x_stored[unit.x_slot][q], unit.x_visit * 32)
                    sp.dma_start(x[:, unit.x_slot, q].rearrange("p c b n -> p (c b n)"),
                                 x_in[bass.ds(unit.number, 1), :, q, :].rearrange("o p n -> (o p) n")
                                 ).then_inc(x_loaded[unit.x_slot][q], 16)

            def load_taps(unit):
                if not (isinstance(unit.number, int) and unit.group < W_SLOTS):
                    sp.wait_ge(quarter_convolved, (unit.number - (W_SLOTS - 1) * UNITS_PER_GROUP) * QUARTERS)
                sp.dma_start(taps[:, unit.w_slot].rearrange("p c t s m -> p (c t s m)"),
                             taps_in[bass.ds(unit.group, 1), :, :].rearrange("o p n -> (o p) n")
                             ).then_inc(taps_loaded[unit.w_slot], 16)

            def store(unit, q):
                sp.wait_ge(quarter_added[unit.g_slot], unit.g_visit * QUARTERS + q + 1)
                for half in range(2):
                    first = half * HALF + HALO_PARTS
                    sp.dma_start(out[bass.ds(unit.number, 1), half * MAIN_PARTS:(half + 1) * MAIN_PARTS, q, :]
                                 .rearrange("o p n -> (o p) n"),
                                 x[first:first + MAIN_PARTS, unit.x_slot, q].rearrange("p c b n -> p (c b n)")
                                 ).then_inc(x_stored[unit.x_slot][q], 16)

            load(Unit(0, 0), range(1))
            sp.dma_start(tap_list[:], tap_list_in).then_inc(constants_loaded, 16)
            sp.dma_start(alpha[:], alpha_in.to_broadcast([P, 1])).then_inc(constants_loaded, 16)
            sp.dma_start(bias[:], bias_in.to_broadcast([P, 1])).then_inc(constants_loaded, 16)
            sp.dma_start(matrices[:], matrices_in).then_inc(constants_loaded, 16)
            load(Unit(0, 0), range(1, QUARTERS))
            load_taps(Unit(0, 0))
            load(Unit(0, 1))
            load(Unit(0, 2))

            def phase(i, k, last=False):
                unit, ahead = Unit(i, k), Unit(i, k + 2)
                if ahead.group_start and not (last and k + 2 >= X_SLOTS):
                    load_taps(ahead)
                store(unit, 0)
                if not (last and k + 3 >= X_SLOTS):
                    load(Unit(i, k + 3))
                for q in range(1, QUARTERS):
                    store(unit, q)

            for k in range(X_SLOTS):
                phase(0, k)
            with sp.Fori(1, LAST) as i:
                for k in range(X_SLOTS):
                    phase(i, k)
            for k in range(X_SLOTS):
                phase(LAST, k, last=True)
            for slot in range(X_SLOTS):
                for q in range(QUARTERS):
                    sp.wait_ge(x_stored[slot][q], 32 * (LAST + 1))

        @block.scalar
        def _(act):
            ROOT_AT = 3

            def scale_taps(unit):
                act.wait_ge(taps_loaded[unit.w_slot], (unit.w_visit + 1) * 16)
                w = taps[:, unit.w_slot].rearrange("p c t s m -> p (c t s m)")
                nc.scalar.activation(w, w, ACT.Copy, scale=tap_scale[:, 0:1]).then_inc(taps_scaled, 1)
                act.wait_ge(taps_scaled, unit.group + 1)
                nc.scalar.activation(taps_high[:, unit.w_slot].rearrange("p c t s m -> p (c t s m)"), w,
                                     ACT.Copy).then_inc(taps_rounded, 1)

            def root(unit):
                act.wait_ge(var_ready, unit.number + 1)
                nc.scalar.activation(std[:], var_ps[:, 0:UNIT_IMAGES], ACT.Sqrt,
                                     bias=eps[:, 0:1]).then_inc(std_ready, 1)

            def normalize(unit, ahead):
                act.wait_ge(coefficients_ready, unit.number + 1)
                wait_unless_zero(act, quarter_added[unit.g_slot], unit.g_visit * QUARTERS)
                for q in range(QUARTERS):
                    if q == ROOT_AT and ahead is not None:
                        root(ahead)
                    for b in range(QUARTER):
                        image = q * QUARTER + b
                        last = nc.scalar.activation(
                            g[:, unit.g_slot, q, :, b * STRIPS:(b + 1) * STRIPS, 1:1 + PATCHES],
                            x_image(unit, image).rearrange("p c (s j) -> p c s j", s=STRIPS),
                            ACT.Identity, scale=rstd[:, unit.g_slot, image:image + 1],
                            bias=shift[:, unit.g_slot, image:image + 1])
                    last.then_inc(normalized, 1)
                    act.wait_ge(normalized, unit.number * QUARTERS + q + 1)
                    for half, strip in ((0, 0), (1, STRIPS - 1)):
                        lanes = slice(half * HALF, half * HALF + HALO_PARTS)
                        last = nc.scalar.activation(
                            g[lanes, unit.g_slot, q, :, strip::STRIPS, 1:1 + PATCHES],
                            zeros[lanes, :].rearrange("p (c b j) -> p c b j", c=GROUP_CH, b=QUARTER), ACT.Copy)
                    last.then_inc(g_ready, 1)
                    if q >= SPLIT:
                        act.wait_ge(g_ready, unit.number * QUARTERS + q + 1)
                        nc.scalar.activation(
                            g_high[:, unit.g_slot, q - SPLIT, :, :, 1:1 + PATCHES].rearrange("p c s j -> p (c s) j"),
                            g[:, unit.g_slot, q, :, :, 1:1 + PATCHES].rearrange("p c s j -> p (c s) j"),
                            ACT.Copy, scale=g_restore[:, 0:1]).then_inc(g_rounded, 1)

            act.wait_ge(bounded_ready, 1)
            nc.scalar.activation(bounded_root[:], bounded[:], ACT.Sqrt).then_inc(bounded_root_ready, 1)
            act.wait_ge(scales_ready, 1)
            scale_taps(Unit(0, 0))
            act.wait_ge(cleared, 6)
            root(Unit(0, 0))
            normalize(Unit(0, 0), Unit(0, 1))

            def phase(i, k, last=False):
                unit = Unit(i, k + 1)
                if unit.group_start:
                    scale_taps(unit)
                normalize(unit, None if last and k + 2 >= X_SLOTS else Unit(i, k + 2))

            for k in range(X_SLOTS):
                phase(0, k)
            with act.Fori(1, LAST) as i:
                for k in range(X_SLOTS):
                    phase(i, k)
            for k in range(X_SLOTS - 1):
                phase(LAST, k, last=True)

        @block.vector
        def _(dve):
            STEPS = 9

            def find_scale():
                done = 0

                def step(instruction):
                    nonlocal done
                    instruction.then_inc(setup_step, 1)
                    done += 1
                    dve.wait_ge(setup_step, done)

                dve.wait_ge(constants_loaded, 64)
                step(nc.vector.tensor_scalar(alpha_tap_list[:], tap_list[:], alpha[0:CHANNELS, 0:1], None, ALU.mult))
                step(nc.vector.tensor_reduce(channel_max[:], alpha_tap_list[:], AXIS.X, ALU.max,
                                             apply_absolute_value=True))
                nc.vector.tensor_scalar(channel_max_diagonal[:], matrices[0:CHANNELS, 2, 0:CHANNELS],
                                        channel_max[:, 0:1], None, ALU.mult).then_inc(channel_max_ready, 1)
                step(nc.vector.tensor_scalar(bias_plus_one[:], bias[:], 1.0, None, ALU.add))
                dve.wait_ge(channel_max_spread, 1)
                step(nc.vector.tensor_reduce(largest[:], var_ps[:, 0:CHANNELS], AXIS.X, ALU.max))
                nc.vector.tensor_scalar(bounded[:], largest[:], 2.0 ** -60, 2.0 ** 100,
                                        ALU.max, ALU.min).then_inc(bounded_ready, 1)
                dve.wait_ge(bounded_root_ready, 1)
                step(nc.vector.tensor_scalar(power[:].bitcast(int32), bounded_root[:].bitcast(int32),
                                             0x7F800000, None, ALU.bitwise_and))
                step(nc.vector.tensor_scalar(r[:], power[:], 2.0 ** -(TAP_BITS // 2), None, ALU.mult))
                nc.vector.tensor_scalar(rstd_scale[:, 0:SPLIT * QUARTER], rstd_scale[:, 0:SPLIT * QUARTER],
                                        r[:, 0:1], None, ALU.mult)
                nc.vector.reciprocal(r_inverse[:], r[:])
                step(nc.vector.tensor_tensor(r_squared[:], r[:], r[:], ALU.mult))
                nc.vector.tensor_scalar(rstd_scale[:, SPLIT * QUARTER:], rstd_scale[:, SPLIT * QUARTER:],
                                        r_squared[:, 0:1], 1.0 / G_SCALE, ALU.mult, ALU.mult)
                nc.vector.tensor_tensor(gate_bias[:], bias_plus_one[:], r_inverse[:], ALU.mult)
                step(nc.vector.reciprocal(r_squared_inverse[:], r_squared[:]))
                nc.vector.tensor_tensor(tap_scale[:], alpha[:], r_squared_inverse[:], ALU.mult)
                nc.vector.tensor_scalar(g_restore[:], r_squared_inverse[:], G_SCALE * G_SCALE, None, ALU.mult)
                nc.vector.tensor_scalar(gate_bias_split[:], r_squared_inverse[:], bias_plus_one[:, 0:1], G_SCALE,
                                        ALU.mult, ALU.mult).then_inc(scales_ready, 1)
                dve.wait_ge(scales_ready, 1)

            def statistics(unit, image):
                q, b = divmod(image, QUARTER)
                if b == 0:
                    dve.wait_ge(x_loaded[unit.x_slot][q], (unit.x_visit + 1) * 16)
                return nc.vector.bn_stats(moments[:, unit.g_slot, image].rearrange("p e n -> p (e n)"),
                                          x_image(unit, image))

            def step(unit, n, instruction, meanwhile=()):
                instruction.then_inc(dve_step, 1)
                for other, image in meanwhile:
                    statistics(other, image)
                dve.wait_ge(dve_step, unit.number * STEPS + n)

            def sum_means(unit, last_image, meanwhile=()):
                step(unit, 1, last_image, meanwhile)
                m = moments[:, unit.g_slot]
                nc.vector.tensor_tensor(mean_sum[:], m[:, :, 0, 1], m[:, :, 1, 1],
                                        ALU.add).then_inc(mean_sum_ready, 1)

            def sum_squares(unit, meanwhile=()):
                dve.wait_ge(mean_ready, unit.number + 1)
                m = moments[:, unit.g_slot]
                mean = mean_ps[:, 0:UNIT_IMAGES].unsqueeze(2).to_broadcast([P, UNIT_IMAGES, 2])
                step(unit, 2, nc.vector.tensor_tensor(offset[:], m[:, :, :, 1], mean, ALU.subtract), meanwhile[0:1])
                step(unit, 3, nc.vector.tensor_tensor(offset_sq[:], offset[:], offset[:], ALU.mult), meanwhile[1:2])
                step(unit, 4, nc.vector.scalar_tensor_tensor(squares[:], offset_sq[:], float(BN_COUNT),
                                                             m[:, :, :, 2], ALU.mult, ALU.add), meanwhile[2:])
                nc.vector.tensor_tensor(square_sum[:], squares[:, :, 0], squares[:, :, 1],
                                        ALU.add).then_inc(square_sum_ready, 1)

            def coefficients(unit, meanwhile=()):
                dve.wait_ge(std_ready, unit.number + 1)
                step(unit, 5, nc.vector.reciprocal(rstd_raw[:], std[:]), meanwhile[0:1])
                step(unit, 6, nc.vector.scalar_tensor_tensor(newton_a[:], var_ps[:, 0:UNIT_IMAGES], EPS, rstd_raw[:],
                                                             ALU.add, ALU.mult), meanwhile[1:2])
                nc.vector.tensor_tensor(rstd_scaled[:], rstd_raw[:], rstd_scale[:], ALU.mult).then_inc(dve_step, 1)
                step(unit, 8, nc.vector.scalar_tensor_tensor(newton_b[:], newton_a[:], -0.5, rstd_raw[:],
                                                             ALU.mult, ALU.mult), meanwhile[2:3])
                step(unit, 9, nc.vector.scalar_tensor_tensor(rstd[:, unit.g_slot], newton_b[:], 1.5, rstd_scaled[:],
                                                             ALU.add, ALU.mult), meanwhile[3:4])
                nc.vector.scalar_tensor_tensor(shift[:, unit.g_slot], mean_ps[:, 0:UNIT_IMAGES], -1.0,
                                               rstd[:, unit.g_slot], ALU.mult, ALU.mult
                                               ).then_inc(coefficients_ready, 1)

            def split(unit, q):
                dve.wait_ge(g_rounded, unit.number * SPLIT_QUARTERS + q - SPLIT + 1)
                nc.vector.scalar_tensor_tensor(
                    g_low[:, q - SPLIT, :, :, 1:1 + PATCHES].rearrange("p c s j -> p (c s) j"),
                    g[:, unit.g_slot, q, :, :, 1:1 + PATCHES].rearrange("p c s j -> p (c s) j"),
                    g_restore[:, 0:1],
                    g_high[:, unit.g_slot, q - SPLIT, :, :, 1:1 + PATCHES].rearrange("p c s j -> p (c s) j"),
                    ALU.mult, ALU.subtract).then_inc(g_split, 1)

            def gate(unit, q):
                slot, _ = unit.psum(q)
                dve.wait_ge(quarter_convolved, unit.number * QUARTERS + q + 1)
                gq = g[:, unit.g_slot, q, :, :, 1:1 + PATCHES].rearrange("p c s j -> p (c s) j")
                product = conv[slot][:, :, :, 0:PATCHES].rearrange("p c s j -> p (c s) j")
                scaled_bias = gate_bias if q < SPLIT else gate_bias_split
                nc.vector.scalar_tensor_tensor(gq, product, scaled_bias[:, 0:1], gq,
                                               ALU.add, ALU.mult).then_inc(quarter_gated[slot], 1)

            nc.vector.memset(zeros[:], 0.0).then_inc(cleared, 1)
            edges = g[:, :, :, :, :, ::PADDED - 1].rearrange("p a q c s j -> p (a q c s) j")
            nc.vector.memset(edges, 0.0).then_inc(cleared, 1)
            edges = g_high[:, :, :, :, :, ::PADDED - 1].rearrange("p a q c s j -> p (a q c s) j")
            nc.vector.memset(edges, 0.0).then_inc(cleared, 1)
            edges = g_low[:, :, :, :, ::PADDED - 1].rearrange("p q c s j -> p (q c s) j")
            nc.vector.memset(edges, 0.0).then_inc(cleared, 1)
            nc.vector.memset(ones[:], 1.0).then_inc(cleared, 1)
            nc.vector.memset(eps[:], EPS).then_inc(cleared, 1)
            nc.vector.memset(rstd_scale[:], 1.0)
            first = Unit(0, 0)
            for image in range(QUARTER):
                statistics(first, image)
            find_scale()
            for image in range(QUARTER, UNIT_IMAGES):
                measured = statistics(first, image)
            sum_means(first, measured)
            sum_squares(first)
            coefficients(first)

            EARLY = 15
            for image in range(EARLY):
                statistics(Unit(0, 1), image)

            def phase(i, k, last=False):
                unit = Unit(i, k)
                if last and k == X_SLOTS - 1:
                    gate(unit, 0)
                    split(unit, 2)
                    split(unit, 3)
                    for q in range(1, QUARTERS):
                        gate(unit, q)
                    return
                ahead = Unit(i, k + 1)
                early = [] if last and k + 2 >= X_SLOTS else [(Unit(i, k + 2), image) for image in range(EARLY)]
                for image in range(EARLY, UNIT_IMAGES):
                    measured = statistics(ahead, image)

                def measure(first, last):
                    for other, image in early[first:last]:
                        statistics(other, image)

                sum_means(ahead, measured, early[0:1])
                measure(1, 2)
                sum_squares(ahead, early[2:5])
                gate(unit, 0)
                split(unit, 2)
                coefficients(ahead, early[5:8])
                gate(unit, 1)
                split(unit, 3)
                measure(8, 9)
                gate(unit, 2)
                measure(9, EARLY)
                gate(unit, 3)

            for k in range(X_SLOTS):
                phase(0, k)
            with dve.Fori(1, LAST) as i:
                for k in range(X_SLOTS):
                    phase(i, k)
            for k in range(X_SLOTS):
                phase(LAST, k, last=True)

        @block.tensor
        def _(pe):
            def average(unit, which, ready, source, target, done):
                pe.wait_ge(ready, unit.number + 1)
                nc.tensor.matmul(target[:, 0:UNIT_IMAGES], matrices[:, which, :], source[:],
                                 start=True, stop=True).then_inc(done, 1)

            def average_means(unit):
                average(unit, 0, mean_sum_ready, mean_sum, mean_ps, mean_ready)

            def average_squares(unit):
                average(unit, 1, square_sum_ready, square_sum, var_ps, var_ready)

            def products(unit, q, c, parts):
                slot, _ = unit.psum(q)
                for n, (weights, moving) in enumerate(parts):
                    for stream in range(2):
                        for half in range(2):
                            j = stream + half
                            last = nc.tensor.matmul(
                                conv[slot][half * HALF:(half + 1) * HALF, c, :, 0:PATCHES],
                                weights[:, half, stream, :], moving[:, :, j:j + PATCHES],
                                start=n == 0 and stream == 0, stop=n == len(parts) - 1 and stream == 1)
                return last

            def convolve(unit, tile):
                q, c = divmod(tile, GROUP_CH)
                slot, held = unit.psum(q)
                if c == 0:
                    wait_unless_zero(pe, quarter_gated[slot], held)
                if q < SPLIT:
                    if c == 0:
                        pe.wait_ge(g_ready, unit.number * QUARTERS + q + 1)
                    last = products(unit, q, c, [(taps[:, unit.w_slot, c], g[:, unit.g_slot, q, c])])
                else:
                    if c == 0:
                        pe.wait_ge(g_split, unit.number * SPLIT_QUARTERS + q - SPLIT + 1)
                    high = g_high[:, unit.g_slot, q - SPLIT, c]
                    last = products(unit, q, c, [(taps_high[:, unit.w_slot, c], high),
                                                 (taps_low[:, unit.w_slot, c], high),
                                                 (taps_high[:, unit.w_slot, c], g_low[:, q - SPLIT, c])])
                if c == GROUP_CH - 1:
                    last.then_inc(quarter_convolved, 1)

            pe.wait_ge(cleared, 5)
            pe.wait_ge(channel_max_ready, 1)
            nc.tensor.matmul(var_ps[:, 0:CHANNELS], ones[:], channel_max_diagonal[:],
                             start=True, stop=True).then_inc(channel_max_spread, 1)
            pe.wait_ge(constants_loaded, 64)
            average_means(Unit(0, 0))
            average_squares(Unit(0, 0))

            def phase(i, k, last=False):
                unit = Unit(i, k)
                ahead = None if last and k == X_SLOTS - 1 else Unit(i, k + 1)
                if unit.group_start:
                    pe.wait_ge(taps_scaled, unit.group + 1)
                for tile in range(TILES):
                    if unit.group_start and tile == SPLIT * GROUP_CH:
                        pe.wait_ge(taps_split, unit.group + 1)
                    convolve(unit, tile)
                    if ahead is not None and tile == 1:
                        average_means(ahead)
                    if ahead is not None and tile == 3:
                        average_squares(ahead)

            for k in range(X_SLOTS):
                phase(0, k)
            with pe.Fori(1, LAST) as i:
                for k in range(X_SLOTS):
                    phase(i, k)
            for k in range(X_SLOTS):
                phase(LAST, k, last=True)

        @block.gpsimd
        def _(pool):
            def split_taps(unit):
                pool.wait_ge(taps_rounded, unit.group + 1)
                nc.gpsimd.tensor_tensor(taps_low[:, unit.w_slot].rearrange("p c t s m -> p (c t s m)"),
                                        taps[:, unit.w_slot].rearrange("p c t s m -> p (c t s m)"),
                                        taps_high[:, unit.w_slot].rearrange("p c t s m -> p (c t s m)"),
                                        ALU.subtract).then_inc(taps_split, 1)

            def add(unit, q):
                slot, held = unit.psum(q)
                pool.wait_ge(quarter_gated[slot], held + 1)
                xq = x[:, unit.x_slot, q].rearrange("p c b (s j) -> p (c b s) j", j=PATCHES)
                tq = g[:, unit.g_slot, q, :, :, 1:1 + PATCHES].rearrange("p c s j -> p (c s) j")
                nc.gpsimd.tensor_tensor(xq, xq, tq, ALU.add).then_inc(quarter_added[unit.g_slot], 1)

            def phase(i, k, last=False):
                ahead = Unit(i, k + 1)
                for q in range(QUARTERS):
                    add(Unit(i, k), q)
                    if q == 1 and ahead.group_start and not (last and k == X_SLOTS - 1):
                        split_taps(ahead)

            split_taps(Unit(0, 0))
            for k in range(X_SLOTS):
                phase(0, k)
            with pool.Fori(1, LAST) as i:
                for k in range(X_SLOTS):
                    phase(i, k)
            for k in range(X_SLOTS):
                phase(LAST, k, last=True)



def _lay_out_x(x):
    import numpy as np
    padded = np.zeros((IMAGES, HEIGHT + 2 * HALO, WIDTH, CHANNELS), x.dtype)
    padded[:, HALO:HALO + HEIGHT] = x

    def rows(first, count):
        at = [HALO + s * ROWS + first for s in range(STRIPS)]
        a = np.stack([padded[:, r:r + count] for r in at], 1)
        return a.reshape(UNITS_PER_GROUP, QUARTERS, QUARTER, STRIPS, count, PATCHES, COLS, GROUPS, GROUP_CH)

    def order(a, row_first):
        a = a.transpose((7, 0, 4, 6, 1, 8, 2, 3, 5) if row_first else (7, 0, 6, 4, 1, 8, 2, 3, 5))
        return a.reshape(UNITS, a.shape[2] * a.shape[3], QUARTERS, GROUP_CH * QUARTER * COLUMNS)

    main = rows(0, ROWS)
    result = np.empty((UNITS, P, QUARTERS, GROUP_CH * QUARTER * COLUMNS), x.dtype)
    result[:, 0:HALO_PARTS] = order(rows(-HALO, HALO), True)
    result[:, HALO_PARTS:HALF] = order(main[..., 0:COLS // 2, :, :], False)
    result[:, HALF:HALF + HALO_PARTS] = order(rows(ROWS, HALO), True)
    result[:, HALF + HALO_PARTS:] = order(main[..., COLS // 2:, :, :], False)
    return result


def _partition_pixels():
    top = [(r - HALO, w, False) for r in range(HALO) for w in range(COLS)]
    left = [(r, w, True) for w in range(COLS // 2) for r in range(ROWS)]
    bottom = [(ROWS + r, w, False) for r in range(HALO) for w in range(COLS)]
    right = [(r, w, True) for w in range(COLS // 2, COLS) for r in range(ROWS)]
    return top + left + bottom + right


def _lay_out_taps(kernel):
    import numpy as np
    pixels = _partition_pixels()
    result = np.zeros((P, 2, 2, HALF, CHANNELS), kernel.dtype)
    for half in range(2):
        for stream in range(2):
            patch = stream + half - 1
            for m in range(HALF):
                row, col, own = pixels[half * HALF + m]
                if not own:
                    continue
                for k, (in_row, in_col, _) in enumerate(pixels):
                    dy, dx = in_row - row + HALO, patch * COLS + in_col - col + HALO
                    if 0 <= dy < TAPS and 0 <= dx < TAPS:
                        result[k, half, stream, m] = kernel[dy, dx]
    result = result.reshape(P, 2, 2, HALF, GROUPS, GROUP_CH).transpose(4, 0, 5, 1, 2, 3)
    return np.ascontiguousarray(result).reshape(GROUPS, P, GROUP_CH * 2 * 2 * HALF)


def _matrices():
    import numpy as np
    result = np.zeros((P, 3, P), np.float32)
    result[:, 2] = np.eye(P, dtype=np.float32)
    for k, (_, _, own) in enumerate(_partition_pixels()):
        if own:
            result[k, 0] = 1.0 / (2 * MAIN_TOTAL)
            result[k, 1] = 1.0 / (2 * MAIN_TOTAL * BN_COUNT)
    return result


def _restore(out):
    import numpy as np
    a = out.reshape(GROUPS, UNITS_PER_GROUP, COLS, ROWS, QUARTERS, GROUP_CH, QUARTER, STRIPS, PATCHES)
    a = a.transpose(1, 4, 6, 7, 3, 8, 2, 0, 5)
    return np.ascontiguousarray(a).reshape(IMAGES, HEIGHT, WIDTH, CHANNELS)


def kernel(x, L0_conv_kernel, L0_conv_alpha, L0_conv_bias):
    import numpy as np
    import concourse.bacc as bacc
    from concourse.bass_utils import run_bass_kernel_spmd

    arrays = {
        "x_in": _lay_out_x(np.asarray(x)),
        "taps_in": _lay_out_taps(np.asarray(L0_conv_kernel)),
        "tap_list_in": np.ascontiguousarray(np.asarray(L0_conv_kernel).reshape(TAPS * TAPS, CHANNELS).T),
        "alpha_in": np.ascontiguousarray(L0_conv_alpha),
        "bias_in": np.ascontiguousarray(L0_conv_bias),
        "matrices_in": _matrices(),
    }
    nc = bacc.Bacc("TRN2", target_bir_lowering=False, num_devices=1)
    ins = [nc.dram_tensor(n, a.shape, mybir.dt.from_np(a.dtype), kind="ExternalInput").ap()
           for n, a in arrays.items()]
    shape = (UNITS, MAIN_TOTAL, QUARTERS, GROUP_CH * QUARTER * COLUMNS)
    out = nc.dram_tensor("out", shape, mybir.dt.float32, kind="ExternalOutput").ap()
    build(nc, *ins, out)
    result = run_bass_kernel_spmd(nc, [arrays], core_ids=[0])
    return _restore(np.asarray(result.results[0]["out"]))
```

```python
from contextlib import ExitStack

import concourse.bass as bass
from concourse import mybir

IMAGES, HEIGHT, WIDTH, CHANNELS = 32, 112, 112, 96
TAPS = 5
HALO = TAPS // 2
GROUPS = 32
GROUP_CH = CHANNELS // GROUPS
EPS = 1e-5

P = 128
COLS = 4
ROWS = P // COLS - 2 * HALO
STRIPS = HEIGHT // ROWS
PATCHES = WIDTH // COLS
HALF = P // 2
HALO_PARTS = HALO * COLS
MAIN_PARTS = HALF - HALO_PARTS

QUARTER = 4
QUARTERS = 4
UNIT_IMAGES = QUARTER * QUARTERS
UNITS = GROUPS * (IMAGES // UNIT_IMAGES)
UNITS_PER_GROUP = IMAGES // UNIT_IMAGES
COLUMNS = STRIPS * PATCHES
STRIPES = QUARTER * STRIPS
PADDED = PATCHES + 2
RUN = 512 // STRIPES

X_SLOTS = 4
G_SLOTS = 2
W_SLOTS = 2
SPLIT = 2
SPLIT_QUARTERS = QUARTERS - SPLIT
TAP_BITS = 12
G_SCALE = 256.0
PSUM_SLOTS = 2
BN = 6
BN_COUNT = GROUP_CH * COLUMNS // 2
MAIN_TOTAL = 2 * MAIN_PARTS


def build(nc, x_in, taps_in, tap_list_in, alpha_in, bias_in, matrices_in, out):
    fp32, fp16, int32 = mybir.dt.float32, mybir.dt.float16, mybir.dt.int32
    AXIS = mybir.AxisListType
    ALU = mybir.AluOpType
    ACT = mybir.ActivationFunctionType

    with ExitStack() as ctx:
        def sb(name, shape, dtype=fp32):
            return ctx.enter_context(nc.sbuf_tensor(name, shape, dtype))

        def sem(name):
            return ctx.enter_context(nc.semaphore(name))

        x = sb("x", [P, X_SLOTS, QUARTERS, GROUP_CH, QUARTER, COLUMNS])
        g = sb("g", [P, G_SLOTS, QUARTERS, GROUP_CH, STRIPES, PADDED])
        taps = sb("taps", [P, W_SLOTS, GROUP_CH, 4, HALF])
        zeros = sb("zeros", [P, GROUP_CH * QUARTER * PATCHES])
        g_high = sb("g_high", [P, G_SLOTS, SPLIT_QUARTERS, GROUP_CH, STRIPES, PADDED], fp16)
        g_low = sb("g_low", [P, SPLIT_QUARTERS, GROUP_CH, STRIPES, PADDED], fp16)
        taps_high = sb("taps_high", [P, W_SLOTS, GROUP_CH, 4, HALF], fp16)
        taps_low = sb("taps_low", [P, W_SLOTS, GROUP_CH, 4, HALF], fp16)
        matrices = sb("matrices", [P, 3, P])
        ones = sb("ones", [CHANNELS, P])
        alpha = sb("alpha", [P, 1])
        bias = sb("bias", [P, 1])
        tap_list = sb("tap_list", [CHANNELS, TAPS * TAPS])
        alpha_tap_list = sb("alpha_tap_list", [CHANNELS, TAPS * TAPS])
        channel_max = sb("channel_max", [CHANNELS, 1])
        channel_max_diagonal = sb("channel_max_diagonal", [CHANNELS, CHANNELS])
        largest = sb("largest", [P, 1])
        bounded = sb("bounded", [P, 1])
        bounded_root = sb("bounded_root", [P, 1])
        power = sb("power", [P, 1])
        r = sb("r", [P, 1])
        r_inverse = sb("r_inverse", [P, 1])
        r_squared = sb("r_squared", [P, 1])
        r_squared_inverse = sb("r_squared_inverse", [P, 1])
        bias_plus_one = sb("bias_plus_one", [P, 1])
        tap_scale = sb("tap_scale", [P, 1])
        gate_bias = sb("gate_bias", [P, 1])
        gate_bias_split = sb("gate_bias_split", [P, 1])
        g_restore = sb("g_restore", [P, 1])
        moments = sb("moments", [P, G_SLOTS, UNIT_IMAGES, 2, BN // 2])
        offset = sb("offset", [P, UNIT_IMAGES, 2])
        squares = sb("squares", [P, UNIT_IMAGES, 2])
        square_sum = sb("square_sum", [P, UNIT_IMAGES])
        eps = sb("eps", [P, 1])
        std = sb("std", [P, UNIT_IMAGES])
        rstd_raw = sb("rstd_raw", [P, UNIT_IMAGES])
        rstd_scaled = sb("rstd_scaled", [P, UNIT_IMAGES])
        rstd = sb("rstd", [P, G_SLOTS, UNIT_IMAGES])
        shift = sb("shift", [P, G_SLOTS, UNIT_IMAGES])

        conv = [ctx.enter_context(nc.psum_tensor(f"conv{n}", [P, GROUP_CH, STRIPES, RUN], fp32))
                for n in range(PSUM_SLOTS)]
        averages = ctx.enter_context(nc.psum_tensor("averages", [P, 2, 256], fp32))
        mean_ps, var_ps = averages[:, 0], averages[:, 1]
        vector_ps = ctx.enter_context(nc.psum_tensor("vector_ps", [P, 32, UNIT_IMAGES], fp32))
        rstd_scale = vector_ps[:, 0]
        newton_a, newton_b = vector_ps[:, 1], vector_ps[:, 2]
        offset_sq = vector_ps[:, 3:5].rearrange("p e n -> p n e")

        x_loaded = [[sem(f"x_loaded{s}_{q}") for q in range(QUARTERS)] for s in range(X_SLOTS)]
        x_stored = [[sem(f"x_stored{s}_{q}") for q in range(QUARTERS)] for s in range(X_SLOTS)]
        taps_loaded = [sem(f"taps_loaded{s}") for s in range(W_SLOTS)]
        constants_loaded = sem("constants_loaded")
        cleared = sem("cleared")
        setup_step = sem("setup_step")
        channel_max_ready = sem("channel_max_ready")
        channel_max_spread = sem("channel_max_spread")
        bounded_ready = sem("bounded_ready")
        bounded_root_ready = sem("bounded_root_ready")
        scales_ready = sem("scales_ready")
        taps_scaled = sem("taps_scaled")
        taps_rounded = sem("taps_rounded")
        taps_split = sem("taps_split")
        moments_ready = sem("moments_ready")
        mean_ready = sem("mean_ready")
        square_sum_ready = sem("square_sum_ready")
        var_ready = sem("var_ready")
        std_ready = sem("std_ready")
        coefficients_ready = sem("coefficients_ready")
        dve_step = sem("dve_step")
        normalized = sem("normalized")
        g_ready = sem("g_ready")
        g_rounded = sem("g_rounded")
        g_split = sem("g_split")
        quarter_convolved = sem("quarter_convolved")
        quarter_gated = [sem(f"quarter_gated{n}") for n in range(PSUM_SLOTS)]
        quarter_added = [sem(f"quarter_added{s}") for s in range(G_SLOTS)]

        class Unit:

            def __init__(self, i, k):
                i, k = i + k // X_SLOTS, k % X_SLOTS
                self.number = i * X_SLOTS + k
                self.x_slot, self.x_visit = k, i
                self.g_slot, self.g_visit = k % G_SLOTS, i * (X_SLOTS // G_SLOTS) + k // G_SLOTS
                self.group_start = k % UNITS_PER_GROUP == 0
                self.w_slot = k // UNITS_PER_GROUP
                self.w_visit = i
                self.group = i * (X_SLOTS // UNITS_PER_GROUP) + k // UNITS_PER_GROUP

            def psum(self, quarter):
                at = self.x_slot * QUARTERS + quarter
                return at % PSUM_SLOTS, self.x_visit * (X_SLOTS * QUARTERS // PSUM_SLOTS) + at // PSUM_SLOTS

        LAST = UNITS // X_SLOTS - 1

        def x_image(unit, image):
            q, b = divmod(image, QUARTER)
            return x[:, unit.x_slot, q, :, b, :]

        def wait_unless_zero(engine, semaphore, count):
            if not (isinstance(count, int) and count == 0):
                engine.wait_ge(semaphore, count)

        block = ctx.enter_context(nc.Block())

        @block.sync
        def _(sp):
            def load(unit, quarters=range(QUARTERS)):
                for q in quarters:
                    wait_unless_zero(sp, x_stored[unit.x_slot][q], unit.x_visit * 32)
                    sp.dma_start(x[:, unit.x_slot, q].rearrange("p c b n -> p (c b n)"),
                                 x_in[bass.ds(unit.number, 1), :, q, :].rearrange("o p n -> (o p) n")
                                 ).then_inc(x_loaded[unit.x_slot][q], 16)

            def load_taps(unit):
                if not (isinstance(unit.number, int) and unit.group < W_SLOTS):
                    sp.wait_ge(quarter_convolved, (unit.number - (W_SLOTS - 1) * UNITS_PER_GROUP) * QUARTERS)
                sp.dma_start(taps[:, unit.w_slot].rearrange("p c b m -> p (c b m)"),
                             taps_in[bass.ds(unit.group, 1), :, :].rearrange("o p n -> (o p) n")
                             ).then_inc(taps_loaded[unit.w_slot], 16)

            def store(unit, q):
                sp.wait_ge(quarter_added[unit.g_slot], unit.g_visit * QUARTERS + q + 1)
                for half in range(2):
                    first = half * HALF + HALO_PARTS
                    sp.dma_start(out[bass.ds(unit.number, 1), half * MAIN_PARTS:(half + 1) * MAIN_PARTS, q, :]
                                 .rearrange("o p n -> (o p) n"),
                                 x[first:first + MAIN_PARTS, unit.x_slot, q].rearrange("p c b n -> p (c b n)")
                                 ).then_inc(x_stored[unit.x_slot][q], 16)

            load(Unit(0, 0), range(1))
            sp.dma_start(tap_list[:], tap_list_in).then_inc(constants_loaded, 16)
            sp.dma_start(alpha[:], alpha_in.to_broadcast([P, 1])).then_inc(constants_loaded, 16)
            sp.dma_start(bias[:], bias_in.to_broadcast([P, 1])).then_inc(constants_loaded, 16)
            sp.dma_start(matrices[:], matrices_in).then_inc(constants_loaded, 16)
            load(Unit(0, 0), range(1, QUARTERS))
            load_taps(Unit(0, 0))
            load(Unit(0, 1))
            load(Unit(0, 2))

            def phase(i, k, last=False):
                unit, ahead = Unit(i, k), Unit(i, k + 2)
                if ahead.group_start and not (last and k + 2 >= X_SLOTS):
                    load_taps(ahead)
                store(unit, 0)
                if not (last and k + 3 >= X_SLOTS):
                    load(Unit(i, k + 3))
                for q in range(1, QUARTERS):
                    store(unit, q)

            for k in range(X_SLOTS):
                phase(0, k)
            with sp.Fori(1, LAST) as i:
                for k in range(X_SLOTS):
                    phase(i, k)
            for k in range(X_SLOTS):
                phase(LAST, k, last=True)
            for slot in range(X_SLOTS):
                for q in range(QUARTERS):
                    sp.wait_ge(x_stored[slot][q], 32 * (LAST + 1))

        @block.scalar
        def _(act):
            def scale_taps(unit):
                act.wait_ge(taps_loaded[unit.w_slot], (unit.w_visit + 1) * 16)
                w = taps[:, unit.w_slot].rearrange("p c b m -> p (c b m)")
                nc.scalar.activation(w, w, ACT.Copy, scale=tap_scale[:, 0:1]).then_inc(taps_scaled, 1)
                act.wait_ge(taps_scaled, unit.group + 1)
                nc.scalar.activation(taps_high[:, unit.w_slot].rearrange("p c b m -> p (c b m)"), w,
                                     ACT.Copy).then_inc(taps_rounded, 1)

            def root(unit):
                act.wait_ge(var_ready, unit.number + 1)
                nc.scalar.activation(std[:], var_ps[:, 0:UNIT_IMAGES], ACT.Sqrt,
                                     bias=eps[:, 0:1]).then_inc(std_ready, 1)

            def normalize(unit, ahead):
                act.wait_ge(coefficients_ready, unit.number + 1)
                wait_unless_zero(act, quarter_added[unit.g_slot], unit.g_visit * QUARTERS)
                for q in range(QUARTERS):
                    for b in range(QUARTER):
                        image = q * QUARTER + b
                        last = nc.scalar.activation(
                            g[:, unit.g_slot, q, :, b * STRIPS:(b + 1) * STRIPS, 1:1 + PATCHES],
                            x_image(unit, image).rearrange("p c (s j) -> p c s j", s=STRIPS),
                            ACT.Identity, scale=rstd[:, unit.g_slot, image:image + 1],
                            bias=shift[:, unit.g_slot, image:image + 1])
                    last.then_inc(normalized, 1)
                    act.wait_ge(normalized, unit.number * QUARTERS + q + 1)
                    for half, strip in ((0, 0), (1, STRIPS - 1)):
                        lanes = slice(half * HALF, half * HALF + HALO_PARTS)
                        last = nc.scalar.activation(
                            g[lanes, unit.g_slot, q, :, strip::STRIPS, 1:1 + PATCHES],
                            zeros[lanes, :].rearrange("p (c b j) -> p c b j", c=GROUP_CH, b=QUARTER), ACT.Copy)
                    last.then_inc(g_ready, 1)
                    if q == QUARTERS - 1 and ahead is not None:
                        root(ahead)
                    if q >= SPLIT:
                        act.wait_ge(g_ready, unit.number * QUARTERS + q + 1)
                        nc.scalar.activation(
                            g_high[:, unit.g_slot, q - SPLIT, :, :, 1:1 + PATCHES].rearrange("p c s j -> p (c s) j"),
                            g[:, unit.g_slot, q, :, :, 1:1 + PATCHES].rearrange("p c s j -> p (c s) j"),
                            ACT.Copy, scale=g_restore[:, 0:1]).then_inc(g_rounded, 1)

            act.wait_ge(bounded_ready, 1)
            nc.scalar.activation(bounded_root[:], bounded[:], ACT.Sqrt).then_inc(bounded_root_ready, 1)
            act.wait_ge(scales_ready, 1)
            scale_taps(Unit(0, 0))
            act.wait_ge(cleared, 6)
            root(Unit(0, 0))
            normalize(Unit(0, 0), Unit(0, 1))

            def phase(i, k, last=False):
                unit = Unit(i, k + 1)
                if unit.group_start:
                    scale_taps(unit)
                normalize(unit, None if last and k + 2 >= X_SLOTS else Unit(i, k + 2))

            for k in range(X_SLOTS):
                phase(0, k)
            with act.Fori(1, LAST) as i:
                for k in range(X_SLOTS):
                    phase(i, k)
            for k in range(X_SLOTS - 1):
                phase(LAST, k, last=True)

        @block.vector
        def _(dve):
            STEPS = 8

            def find_scale():
                done = 0

                def step(instruction):
                    nonlocal done
                    instruction.then_inc(setup_step, 1)
                    done += 1
                    dve.wait_ge(setup_step, done)

                dve.wait_ge(constants_loaded, 64)
                step(nc.vector.tensor_scalar(alpha_tap_list[:], tap_list[:], alpha[0:CHANNELS, 0:1], None, ALU.mult))
                step(nc.vector.tensor_reduce(channel_max[:], alpha_tap_list[:], AXIS.X, ALU.max,
                                             apply_absolute_value=True))
                nc.vector.tensor_scalar(channel_max_diagonal[:], matrices[0:CHANNELS, 2, 0:CHANNELS],
                                        channel_max[:, 0:1], None, ALU.mult).then_inc(channel_max_ready, 1)
                step(nc.vector.tensor_scalar(bias_plus_one[:], bias[:], 1.0, None, ALU.add))
                dve.wait_ge(channel_max_spread, 1)
                step(nc.vector.tensor_reduce(largest[:], var_ps[:, 0:CHANNELS], AXIS.X, ALU.max))
                nc.vector.tensor_scalar(bounded[:], largest[:], 2.0 ** -60, 2.0 ** 100,
                                        ALU.max, ALU.min).then_inc(bounded_ready, 1)
                dve.wait_ge(bounded_root_ready, 1)
                step(nc.vector.tensor_scalar(power[:].bitcast(int32), bounded_root[:].bitcast(int32),
                                             0x7F800000, None, ALU.bitwise_and))
                step(nc.vector.tensor_scalar(r[:], power[:], 2.0 ** -(TAP_BITS // 2), None, ALU.mult))
                nc.vector.tensor_scalar(rstd_scale[:, 0:SPLIT * QUARTER], rstd_scale[:, 0:SPLIT * QUARTER],
                                        r[:, 0:1], None, ALU.mult)
                nc.vector.reciprocal(r_inverse[:], r[:])
                step(nc.vector.tensor_tensor(r_squared[:], r[:], r[:], ALU.mult))
                nc.vector.tensor_scalar(rstd_scale[:, SPLIT * QUARTER:], rstd_scale[:, SPLIT * QUARTER:],
                                        r_squared[:, 0:1], 1.0 / G_SCALE, ALU.mult, ALU.mult)
                nc.vector.tensor_tensor(gate_bias[:], bias_plus_one[:], r_inverse[:], ALU.mult)
                step(nc.vector.reciprocal(r_squared_inverse[:], r_squared[:]))
                nc.vector.tensor_tensor(tap_scale[:], alpha[:], r_squared_inverse[:], ALU.mult)
                nc.vector.tensor_scalar(g_restore[:], r_squared_inverse[:], G_SCALE * G_SCALE, None, ALU.mult)
                nc.vector.tensor_scalar(gate_bias_split[:], r_squared_inverse[:], bias_plus_one[:, 0:1], G_SCALE,
                                        ALU.mult, ALU.mult).then_inc(scales_ready, 1)
                dve.wait_ge(scales_ready, 1)

            def statistics(unit, image):
                q, b = divmod(image, QUARTER)
                if b == 0:
                    dve.wait_ge(x_loaded[unit.x_slot][q], (unit.x_visit + 1) * 16)
                return nc.vector.bn_stats(moments[:, unit.g_slot, image].rearrange("p e n -> p (e n)"),
                                          x_image(unit, image))

            def step_done(unit, n):
                dve.wait_ge(dve_step, unit.number * STEPS + n)


            def subtract_mean(unit):
                dve.wait_ge(mean_ready, unit.number + 1)
                nc.vector.tensor_tensor(offset[:], moments[:, unit.g_slot, :, :, 1],
                                        mean_ps[:, 0:UNIT_IMAGES].unsqueeze(2).to_broadcast([P, UNIT_IMAGES, 2]),
                                        ALU.subtract).then_inc(dve_step, 1)

            def square_offsets(unit):
                step_done(unit, 1)
                nc.vector.tensor_tensor(offset_sq, offset[:], offset[:], ALU.mult).then_inc(dve_step, 1)

            def add_own_squares(unit):
                step_done(unit, 2)
                nc.vector.scalar_tensor_tensor(squares[:], offset_sq, float(BN_COUNT),
                                               moments[:, unit.g_slot, :, :, 2], ALU.mult, ALU.add
                                               ).then_inc(dve_step, 1)

            def sum_squares(unit):
                step_done(unit, 3)
                nc.vector.tensor_tensor(square_sum[:], squares[:, :, 0], squares[:, :, 1],
                                        ALU.add).then_inc(square_sum_ready, 1)


            def invert_root(unit):
                dve.wait_ge(std_ready, unit.number + 1)
                nc.vector.reciprocal(rstd_raw[:], std[:]).then_inc(dve_step, 1)

            def newton_product(unit):
                step_done(unit, 4)
                nc.vector.scalar_tensor_tensor(newton_a, var_ps[:, 0:UNIT_IMAGES], EPS, rstd_raw[:],
                                               ALU.add, ALU.mult).then_inc(dve_step, 1)

            def scale_rstd(unit):
                nc.vector.tensor_tensor(rstd_scaled[:], rstd_raw[:], rstd_scale, ALU.mult).then_inc(dve_step, 1)

            def newton_correction(unit):
                step_done(unit, 5)
                nc.vector.scalar_tensor_tensor(newton_b, newton_a, -0.5, rstd_raw[:],
                                               ALU.mult, ALU.mult).then_inc(dve_step, 1)

            def correct_rstd(unit):
                step_done(unit, 7)
                nc.vector.scalar_tensor_tensor(rstd[:, unit.g_slot], newton_b, 1.5, rstd_scaled[:],
                                               ALU.add, ALU.mult).then_inc(dve_step, 1)

            def find_shift(unit):
                step_done(unit, 8)
                nc.vector.scalar_tensor_tensor(shift[:, unit.g_slot], mean_ps[:, 0:UNIT_IMAGES], -1.0,
                                               rstd[:, unit.g_slot], ALU.mult, ALU.mult
                                               ).then_inc(coefficients_ready, 1)

            def split(unit, q):
                dve.wait_ge(g_rounded, unit.number * SPLIT_QUARTERS + q - SPLIT + 1)
                nc.vector.scalar_tensor_tensor(
                    g_low[:, q - SPLIT, :, :, 1:1 + PATCHES].rearrange("p c s j -> p (c s) j"),
                    g[:, unit.g_slot, q, :, :, 1:1 + PATCHES].rearrange("p c s j -> p (c s) j"),
                    g_restore[:, 0:1],
                    g_high[:, unit.g_slot, q - SPLIT, :, :, 1:1 + PATCHES].rearrange("p c s j -> p (c s) j"),
                    ALU.mult, ALU.subtract).then_inc(g_split, 1)

            def gate(unit, q):
                slot, _ = unit.psum(q)
                dve.wait_ge(quarter_convolved, unit.number * QUARTERS + q + 1)
                gq = g[:, unit.g_slot, q, :, :, 1:1 + PATCHES].rearrange("p c s j -> p (c s) j")
                product = conv[slot][:, :, :, 0:PATCHES].rearrange("p c s j -> p (c s) j")
                scaled_bias = gate_bias if q < SPLIT else gate_bias_split
                nc.vector.scalar_tensor_tensor(gq, product, scaled_bias[:, 0:1], gq,
                                               ALU.add, ALU.mult).then_inc(quarter_gated[slot], 1)

            nc.vector.memset(zeros[:], 0.0).then_inc(cleared, 1)
            edges = g[:, :, :, :, :, ::PADDED - 1].rearrange("p a q c s j -> p (a q c s) j")
            nc.vector.memset(edges, 0.0).then_inc(cleared, 1)
            edges = g_high[:, :, :, :, :, ::PADDED - 1].rearrange("p a q c s j -> p (a q c s) j")
            nc.vector.memset(edges, 0.0).then_inc(cleared, 1)
            edges = g_low[:, :, :, :, ::PADDED - 1].rearrange("p q c s j -> p (q c s) j")
            nc.vector.memset(edges, 0.0).then_inc(cleared, 1)
            nc.vector.memset(ones[:], 1.0).then_inc(cleared, 1)
            nc.vector.memset(eps[:], EPS).then_inc(cleared, 1)
            nc.vector.memset(rstd_scale, 1.0)
            first = Unit(0, 0)
            for image in range(QUARTER):
                statistics(first, image)
            find_scale()
            for image in range(QUARTER, UNIT_IMAGES):
                measured = statistics(first, image)
            measured.then_inc(moments_ready, 1)
            for chain_step in (subtract_mean, square_offsets, add_own_squares, sum_squares, invert_root,
                               newton_product, scale_rstd, newton_correction, correct_rstd, find_shift):
                chain_step(first)

            EARLY = 15
            for image in range(EARLY):
                statistics(Unit(0, 1), image)

            def phase(i, k, last=False):
                unit = Unit(i, k)
                if last and k == X_SLOTS - 1:
                    gate(unit, 0)
                    split(unit, 2)
                    split(unit, 3)
                    for q in range(1, QUARTERS):
                        gate(unit, q)
                    q = QUARTERS - 1
                    slot, held = unit.psum(q)
                    dve.wait_ge(quarter_gated[slot], held + 1)
                    dve.wait_ge(quarter_added[unit.g_slot], unit.g_visit * QUARTERS + q)
                    xq = x[:, unit.x_slot, q].rearrange("p c b (s j) -> p (c b s) j", j=PATCHES)
                    tq = g[:, unit.g_slot, q, :, :, 1:1 + PATCHES].rearrange("p c s j -> p (c s) j")
                    nc.vector.tensor_tensor(xq, xq, tq, ALU.add).then_inc(quarter_added[unit.g_slot], 1)
                    return
                ahead = Unit(i, k + 1)
                early = [] if last and k + 2 >= X_SLOTS else [(Unit(i, k + 2), image) for image in range(EARLY)]
                for image in range(EARLY, UNIT_IMAGES):
                    measured = statistics(ahead, image)
                measured.then_inc(moments_ready, 1)

                def measure(first, last):
                    for other, image in early[first:last]:
                        statistics(other, image)

                measure(0, 3)
                subtract_mean(ahead)
                measure(3, 4)
                square_offsets(ahead)
                measure(4, 5)
                add_own_squares(ahead)
                measure(5, 6)
                sum_squares(ahead)
                gate(unit, 0)
                split(unit, 2)
                invert_root(ahead)
                measure(6, 7)
                newton_product(ahead)
                scale_rstd(ahead)
                newton_correction(ahead)
                correct_rstd(ahead)
                measure(7, 8)
                find_shift(ahead)
                gate(unit, 1)
                split(unit, 3)
                measure(8, 9)
                gate(unit, 2)
                measure(9, 15)
                gate(unit, 3)

            for k in range(X_SLOTS):
                phase(0, k)
            with dve.Fori(1, LAST) as i:
                for k in range(X_SLOTS):
                    phase(i, k)
            for k in range(X_SLOTS):
                phase(LAST, k, last=True)

        @block.tensor
        def _(pe):

            def average_means(unit):
                pe.wait_ge(moments_ready, unit.number + 1)
                for parity in range(2):
                    product = nc.tensor.matmul(mean_ps[:, 0:UNIT_IMAGES], matrices[:, 0, :],
                                               moments[:, unit.g_slot, :, parity, 1],
                                               start=parity == 0, stop=parity == 1)
                product.then_inc(mean_ready, 1)

            def average_squares(unit):
                pe.wait_ge(square_sum_ready, unit.number + 1)
                nc.tensor.matmul(var_ps[:, 0:UNIT_IMAGES], matrices[:, 1, :], square_sum[:],
                                 start=True, stop=True).then_inc(var_ready, 1)

            def multiply_own(unit, q, c, weights, moving, first=True):
                slot, _ = unit.psum(q)
                nc.tensor.matmul(conv[slot][:, c, :, 0:PATCHES], weights[:, c, 1:3].rearrange("p b m -> p (b m)"),
                                 moving[:, c, :, 1:1 + PATCHES], start=first, stop=False)

            def multiply_neighbours(unit, q, c, weights, moving, last=True):
                slot, _ = unit.psum(q)
                for half in range(2):
                    product = nc.tensor.matmul(conv[slot][half * HALF:(half + 1) * HALF, c, :, 0:PATCHES],
                                               weights[:, c, 3 * half], moving[:, c, :, 2 * half:2 * half + PATCHES],
                                               start=False, stop=last)
                return product

            def convolve(unit, q, between=()):
                slot, held = unit.psum(q)
                wait_unless_zero(pe, quarter_gated[slot], held)
                pe.wait_ge(g_ready, unit.number * QUARTERS + q + 1)
                operands = taps[:, unit.w_slot], g[:, unit.g_slot, q]
                for c in range(GROUP_CH):
                    multiply_own(unit, q, c, *operands)
                for c in range(GROUP_CH):
                    for at, run in between:
                        if at == c:
                            run()
                    product = multiply_neighbours(unit, q, c, *operands)
                product.then_inc(quarter_convolved, 1)

            def convolve_split(unit, q):
                slot, held = unit.psum(q)
                wait_unless_zero(pe, quarter_gated[slot], held)
                pe.wait_ge(g_split, unit.number * SPLIT_QUARTERS + q - SPLIT + 1)
                weights_high, weights_low = taps_high[:, unit.w_slot], taps_low[:, unit.w_slot]
                high, low = g_high[:, unit.g_slot, q - SPLIT], g_low[:, q - SPLIT]
                pairs = (weights_high, high), (weights_low, high), (weights_high, low)
                for c in range(GROUP_CH):
                    for n, pair in enumerate(pairs):
                        multiply_own(unit, q, c, *pair, first=n == 0)
                        product = multiply_neighbours(unit, q, c, *pair, last=n == len(pairs) - 1)
                product.then_inc(quarter_convolved, 1)

            pe.wait_ge(cleared, 5)
            pe.wait_ge(channel_max_ready, 1)
            nc.tensor.matmul(var_ps[:, 0:CHANNELS], ones[:], channel_max_diagonal[:],
                             start=True, stop=True).then_inc(channel_max_spread, 1)
            pe.wait_ge(constants_loaded, 64)
            average_means(Unit(0, 0))
            average_squares(Unit(0, 0))

            def phase(i, k, last=False):
                unit = Unit(i, k)
                ahead = None if last and k == X_SLOTS - 1 else Unit(i, k + 1)
                if unit.group_start:
                    pe.wait_ge(taps_scaled, unit.group + 1)
                convolve(unit, 0, [] if ahead is None else [(1, lambda: average_means(ahead))])
                convolve(unit, 1, [] if ahead is None else [(0, lambda: average_squares(ahead))])
                if unit.group_start:
                    pe.wait_ge(taps_split, unit.group + 1)
                for q in range(SPLIT, QUARTERS):
                    convolve_split(unit, q)

            for k in range(X_SLOTS):
                phase(0, k)
            with pe.Fori(1, LAST) as i:
                for k in range(X_SLOTS):
                    phase(i, k)
            for k in range(X_SLOTS):
                phase(LAST, k, last=True)

        @block.gpsimd
        def _(pool):
            def split_taps(unit):
                pool.wait_ge(taps_rounded, unit.group + 1)
                nc.gpsimd.tensor_tensor(taps_low[:, unit.w_slot].rearrange("p c b m -> p (c b m)"),
                                        taps[:, unit.w_slot].rearrange("p c b m -> p (c b m)"),
                                        taps_high[:, unit.w_slot].rearrange("p c b m -> p (c b m)"),
                                        ALU.subtract).then_inc(taps_split, 1)

            def add(unit, q):
                slot, held = unit.psum(q)
                pool.wait_ge(quarter_gated[slot], held + 1)
                xq = x[:, unit.x_slot, q].rearrange("p c b (s j) -> p (c b s) j", j=PATCHES)
                tq = g[:, unit.g_slot, q, :, :, 1:1 + PATCHES].rearrange("p c s j -> p (c s) j")
                nc.gpsimd.tensor_tensor(xq, xq, tq, ALU.add).then_inc(quarter_added[unit.g_slot], 1)

            def phase(i, k, last=False):
                ahead = Unit(i, k + 1)
                for q in range(QUARTERS):
                    if last and k == X_SLOTS - 1 and q == QUARTERS - 1:
                        return
                    add(Unit(i, k), q)
                    if q == 1 and ahead.group_start and not (last and k == X_SLOTS - 1):
                        split_taps(ahead)

            split_taps(Unit(0, 0))
            for k in range(X_SLOTS):
                phase(0, k)
            with pool.Fori(1, LAST) as i:
                for k in range(X_SLOTS):
                    phase(i, k)
            for k in range(X_SLOTS):
                phase(LAST, k, last=True)



def _lay_out_x(x):
    import numpy as np
    padded = np.zeros((IMAGES, HEIGHT + 2 * HALO, WIDTH, CHANNELS), x.dtype)
    padded[:, HALO:HALO + HEIGHT] = x

    def rows(first, count):
        at = [HALO + s * ROWS + first for s in range(STRIPS)]
        a = np.stack([padded[:, r:r + count] for r in at], 1)
        return a.reshape(UNITS_PER_GROUP, QUARTERS, QUARTER, STRIPS, count, PATCHES, COLS, GROUPS, GROUP_CH)

    def order(a, row_first):
        a = a.transpose((7, 0, 4, 6, 1, 8, 2, 3, 5) if row_first else (7, 0, 6, 4, 1, 8, 2, 3, 5))
        return a.reshape(UNITS, a.shape[2] * a.shape[3], QUARTERS, GROUP_CH * QUARTER * COLUMNS)

    main = rows(0, ROWS)
    result = np.empty((UNITS, P, QUARTERS, GROUP_CH * QUARTER * COLUMNS), x.dtype)
    result[:, 0:HALO_PARTS] = order(rows(-HALO, HALO), True)
    result[:, HALO_PARTS:HALF] = order(main[..., 0:COLS // 2, :, :], False)
    result[:, HALF:HALF + HALO_PARTS] = order(rows(ROWS, HALO), True)
    result[:, HALF + HALO_PARTS:] = order(main[..., COLS // 2:, :, :], False)
    return result


def _partition_pixels():
    top = [(r - HALO, w, False) for r in range(HALO) for w in range(COLS)]
    left = [(r, w, True) for w in range(COLS // 2) for r in range(ROWS)]
    bottom = [(ROWS + r, w, False) for r in range(HALO) for w in range(COLS)]
    right = [(r, w, True) for w in range(COLS // 2, COLS) for r in range(ROWS)]
    return top + left + bottom + right


def _lay_out_taps(kernel):
    import numpy as np
    pixels = _partition_pixels()
    result = np.zeros((P, 2, 2, HALF, CHANNELS), kernel.dtype)
    for half in range(2):
        for stream in range(2):
            patch = stream + half - 1
            for m in range(HALF):
                row, col, own = pixels[half * HALF + m]
                if not own:
                    continue
                for k, (in_row, in_col, _) in enumerate(pixels):
                    dy, dx = in_row - row + HALO, patch * COLS + in_col - col + HALO
                    if 0 <= dy < TAPS and 0 <= dx < TAPS:
                        result[k, half, stream, m] = kernel[dy, dx]
    result = result.reshape(P, 2, 2, HALF, GROUPS, GROUP_CH).transpose(4, 0, 5, 1, 2, 3)
    return np.ascontiguousarray(result).reshape(GROUPS, P, GROUP_CH * 2 * 2 * HALF)


def _matrices():
    import numpy as np
    result = np.zeros((P, 3, P), np.float32)
    result[:, 2] = np.eye(P, dtype=np.float32)
    for k, (_, _, own) in enumerate(_partition_pixels()):
        if own:
            result[k, 0] = 1.0 / (2 * MAIN_TOTAL)
            result[k, 1] = 1.0 / (2 * MAIN_TOTAL * BN_COUNT)
    return result


def _restore(out):
    import numpy as np
    a = out.reshape(GROUPS, UNITS_PER_GROUP, COLS, ROWS, QUARTERS, GROUP_CH, QUARTER, STRIPS, PATCHES)
    a = a.transpose(1, 4, 6, 7, 3, 8, 2, 0, 5)
    return np.ascontiguousarray(a).reshape(IMAGES, HEIGHT, WIDTH, CHANNELS)


def kernel(x, L0_conv_kernel, L0_conv_alpha, L0_conv_bias):
    import numpy as np
    import concourse.bacc as bacc
    from concourse.bass_utils import run_bass_kernel_spmd

    arrays = {
        "x_in": _lay_out_x(np.asarray(x)),
        "taps_in": _lay_out_taps(np.asarray(L0_conv_kernel)),
        "tap_list_in": np.ascontiguousarray(np.asarray(L0_conv_kernel).reshape(TAPS * TAPS, CHANNELS).T),
        "alpha_in": np.ascontiguousarray(L0_conv_alpha),
        "bias_in": np.ascontiguousarray(L0_conv_bias),
        "matrices_in": _matrices(),
    }
    nc = bacc.Bacc("TRN2", target_bir_lowering=False, num_devices=1)
    ins = [nc.dram_tensor(n, a.shape, mybir.dt.from_np(a.dtype), kind="ExternalInput").ap()
           for n, a in arrays.items()]
    shape = (UNITS, MAIN_TOTAL, QUARTERS, GROUP_CH * QUARTER * COLUMNS)
    out = nc.dram_tensor("out", shape, mybir.dt.float32, kind="ExternalOutput").ap()
    build(nc, *ins, out)
    result = run_bass_kernel_spmd(nc, [arrays], core_ids=[0])
    return _restore(np.asarray(result.results[0]["out"]))
```
